# Optimizing a Trainium2 kernel written in Bass

```python
import numpy as np
import jax
import jax.numpy as jnp

def _softmax(x, axis=-1):
    return jax.nn.softmax(x, axis=axis)

def _gelu(x):
    return jax.nn.gelu(x, approximate=True)

def _silu(x):
    return jax.nn.silu(x)

def _sigmoid(x):
    return jax.nn.sigmoid(x)

def _layernorm(x, axis=-1, eps=1e-05):
    m = jnp.mean(x, axis=axis, keepdims=True)
    v = jnp.var(x, axis=axis, keepdims=True)
    return (x - m) / jnp.sqrt(v + eps)

def _scatter_add(tgt, idx, src, axis=0):
    return tgt.at[idx].add(src)

def _segment_sum(src, seg, n):
    return jax.ops.segment_sum(src, seg, n)
kernel_name = 'mk_gps_d1_gnn_r32_7b92bc'

def setup_inputs(seed: int=0):
    np.random.seed(seed)
    _w = jnp.asarray

    def _rec_inputs():
        import jax
        import jax.numpy as jnp
        _gk = jax.random.key(seed)
        x = -0.0002117 + 1 * jax.random.normal(jax.random.fold_in(_gk, 1), (3125, 256), jnp.float32)
        _s = jax.random.randint(jax.random.fold_in(_gk, 2), (25000,), 0, 3125, jnp.int32)
        _d = jax.random.randint(jax.random.fold_in(_gk, 3), (25000,), 0, 3125, jnp.int32)
        _loop = jnp.arange(3125, dtype=jnp.int32)
        src = jnp.concatenate([_s, _d, _loop])
        dst = jnp.concatenate([_d, _s, _loop])
        _o = jnp.argsort(dst, stable=True)
        src = src[_o]
        dst = dst[_o]
        return (x, src, dst)
    x, src, dst = _rec_inputs()

    def _L0_gnn_setup():
        import jax, jax.numpy as jnp
        import numpy as np
        N_NODES = 3125

        def sage_conv(x, edge_index, Wl, bl, Wr):
            src, dst = (edge_index[0], edge_index[1])
            msg = x[src]
            agg = jax.ops.segment_sum(msg, dst, num_segments=N_NODES)
            cnt = jax.ops.segment_sum(jnp.ones((edge_index.shape[1],), x.dtype), dst, num_segments=N_NODES)
            agg = agg / jnp.maximum(cnt, 1.0)[:, None]
            return agg @ Wl.T + bl + x @ Wr.T
        key = jax.random.key(seed)
        ks = jax.random.split(key, 8)
        d_in, d_hid, d_out, E = (256, 512, 256, 10000)
        s = lambda k, shape, fan: jax.random.normal(k, shape, jnp.float32) * (1.0 / np.sqrt(fan))
        return {'x': jax.random.normal(ks[0], (N_NODES, d_in), jnp.float32), 'edge_index': jax.random.randint(ks[1], (2, E), 0, N_NODES, dtype=jnp.int64), 'W1l': s(ks[2], (d_hid, d_in), d_in), 'b1l': jnp.zeros((d_hid,), jnp.float32), 'W1r': s(ks[3], (d_hid, d_in), d_in), 'W2l': s(ks[4], (d_out, d_hid), d_hid), 'b2l': jnp.zeros((d_out,), jnp.float32), 'W2r': s(ks[5], (d_out, d_hid), d_hid)}
    _L0_gnn_all = _L0_gnn_setup()
    _L0_gnn_in = {k: v for k, v in _L0_gnn_all.items() if k in ('W1l', 'b1l', 'W1r', 'W2l', 'b2l', 'W2r')}
    del _L0_gnn_all

    def _L0_mix_setup():
        import jax, jax.numpy as jnp
        import numpy as np
        D_MODEL = 256
        NUM_HEADS = 8
        DEPTH = D_MODEL // NUM_HEADS
        B, L = (32, 128)

        def _feature_map(x):
            return jax.nn.elu(x) + 1.0
        key = jax.random.key(seed)
        ks = jax.random.split(key, 9)
        sc = 1.0 / np.sqrt(D_MODEL)
        return {'x': jax.random.normal(ks[0], (B, L, D_MODEL), dtype=jnp.float32), 'wq': jax.random.normal(ks[1], (D_MODEL, D_MODEL), dtype=jnp.float32) * sc, 'bq': jnp.zeros((D_MODEL,), dtype=jnp.float32), 'wk': jax.random.normal(ks[2], (D_MODEL, D_MODEL), dtype=jnp.float32) * sc, 'bk': jnp.zeros((D_MODEL,), dtype=jnp.float32), 'wv': jax.random.normal(ks[3], (D_MODEL, D_MODEL), dtype=jnp.float32) * sc, 'bv': jnp.zeros((D_MODEL,), dtype=jnp.float32), 'wo': jax.random.normal(ks[4], (D_MODEL, D_MODEL), dtype=jnp.float32) * sc, 'bo': jnp.zeros((D_MODEL,), dtype=jnp.float32)}
    _L0_mix_all = _L0_mix_setup()
    _L0_mix_in = {k: v for k, v in _L0_mix_all.items() if k in ('wq', 'bq', 'wk', 'bk', 'wv', 'bv', 'wo', 'bo')}
    del _L0_mix_all

    def _L0_ffn_setup():
        import jax, jax.numpy as jnp
        import numpy as np
        TOP_K = 2
        key = jax.random.key(seed)
        ks = jax.random.split(key, 4)
        B, L, D, H, E = (8, 128, 256, 1024, 8)
        s = 0.02
        return {'x': jax.random.normal(ks[0], (B, L, D), jnp.float32), 'Wg': jax.random.normal(ks[1], (D, E), jnp.float32) * s, 'bg': jnp.zeros((E,), jnp.float32), 'W1': jax.random.normal(ks[2], (E, D, H), jnp.float32) * s, 'b1': jnp.zeros((E, H), jnp.float32), 'W2': jax.random.normal(ks[3], (E, H, D), jnp.float32) * s, 'b2': jnp.zeros((E, D), jnp.float32)}
    _L0_ffn_all = _L0_ffn_setup()
    _L0_ffn_in = {k: v for k, v in _L0_ffn_all.items() if k in ('Wg', 'bg', 'W1', 'b1', 'W2', 'b2')}
    del _L0_ffn_all
    return {'x': x, 'src': src, 'dst': dst, 'L0_gnn_W1l': _L0_gnn_in['W1l'], 'L0_gnn_b1l': _L0_gnn_in['b1l'], 'L0_gnn_W1r': _L0_gnn_in['W1r'], 'L0_gnn_W2l': _L0_gnn_in['W2l'], 'L0_gnn_b2l': _L0_gnn_in['b2l'], 'L0_gnn_W2r': _L0_gnn_in['W2r'], 'L0_mix_wq': _L0_mix_in['wq'], 'L0_mix_bq': _L0_mix_in['bq'], 'L0_mix_wk': _L0_mix_in['wk'], 'L0_mix_bk': _L0_mix_in['bk'], 'L0_mix_wv': _L0_mix_in['wv'], 'L0_mix_bv': _L0_mix_in['bv'], 'L0_mix_wo': _L0_mix_in['wo'], 'L0_mix_bo': _L0_mix_in['bo'], 'L0_ffn_Wg': _L0_ffn_in['Wg'], 'L0_ffn_bg': _L0_ffn_in['bg'], 'L0_ffn_W1': _L0_ffn_in['W1'], 'L0_ffn_b1': _L0_ffn_in['b1'], 'L0_ffn_W2': _L0_ffn_in['W2'], 'L0_ffn_b2': _L0_ffn_in['b2']}

def reference(x, src, dst, L0_gnn_W1l, L0_gnn_b1l, L0_gnn_W1r, L0_gnn_W2l, L0_gnn_b2l, L0_gnn_W2r, L0_mix_wq, L0_mix_bq, L0_mix_wk, L0_mix_bk, L0_mix_wv, L0_mix_bv, L0_mix_wo, L0_mix_bo, L0_ffn_Wg, L0_ffn_bg, L0_ffn_W1, L0_ffn_b1, L0_ffn_W2, L0_ffn_b2):
    import jax
    import jax.numpy as jnp

    def _L0_gnn_ref(x, edge_index, W1l, b1l, W1r, W2l, b2l, W2r):
        import jax, jax.numpy as jnp
        import numpy as np
        N_NODES = 3125

        def sage_conv(x, edge_index, Wl, bl, Wr):
            src, dst = (edge_index[0], edge_index[1])
            msg = x[src]
            agg = jax.ops.segment_sum(msg, dst, num_segments=N_NODES)
            cnt = jax.ops.segment_sum(jnp.ones((edge_index.shape[1],), x.dtype), dst, num_segments=N_NODES)
            agg = agg / jnp.maximum(cnt, 1.0)[:, None]
            return agg @ Wl.T + bl + x @ Wr.T
        h = sage_conv(x, edge_index, W1l, b1l, W1r)
        h = jax.nn.relu(h)
        out = sage_conv(h, edge_index, W2l, b2l, W2r)
        return out

    def _L0_mix_ref(x, wq, bq, wk, bk, wv, bv, wo, bo):
        import jax, jax.numpy as jnp
        import numpy as np
        D_MODEL = 256
        NUM_HEADS = 8
        DEPTH = D_MODEL // NUM_HEADS
        B, L = (32, 128)

        def _feature_map(x):
            return jax.nn.elu(x) + 1.0
        b, l, _ = x.shape
        q = (x @ wq + bq).reshape(b, l, NUM_HEADS, DEPTH)
        k = (x @ wk + bk).reshape(b, l, NUM_HEADS, DEPTH)
        v = (x @ wv + bv).reshape(b, l, NUM_HEADS, DEPTH)
        q = _feature_map(q)
        k = _feature_map(k)
        kv = jnp.einsum('blhd,blhe->bhde', k, v)
        k_sum = jnp.sum(k, axis=1)
        qkv = jnp.einsum('blhd,bhde->blhe', q, kv)
        normalizer = jnp.einsum('blhd,bhd->blh', q, k_sum) + 1e-06
        out = qkv / normalizer[..., None]
        out = out.reshape(b, l, D_MODEL)
        return out @ wo + bo

    def _L0_ffn_ref(x, Wg, bg, W1, b1, W2, b2):
        import jax, jax.numpy as jnp
        import numpy as np
        TOP_K = 2
        B, L, D = x.shape
        E = W1.shape[0]
        xf = x.reshape(-1, D)
        gate_logits = xf @ Wg + bg
        top_w, top_i = jax.lax.top_k(gate_logits, TOP_K)
        top_w = jax.nn.softmax(top_w, axis=-1)
        w_dense = jnp.sum(jax.nn.one_hot(top_i, E, dtype=xf.dtype) * top_w[..., None], axis=1)
        out = jnp.zeros_like(xf)
        for e in range(E):
            h = jax.nn.gelu(xf @ W1[e] + b1[e], approximate=False)
            out = out + w_dense[:, e:e + 1] * (h @ W2[e] + b2[e])
        return out.reshape(B, L, D)
    edge_index = jnp.stack([src, dst])
    xn = _layernorm(x, axis=-1)
    x = x + _L0_gnn_ref(xn, edge_index, L0_gnn_W1l, L0_gnn_b1l, L0_gnn_W1r, L0_gnn_W2l, L0_gnn_b2l, L0_gnn_W2r) + _L0_mix_ref(xn[None], L0_mix_wq, L0_mix_bq, L0_mix_wk, L0_mix_bk, L0_mix_wv, L0_mix_bv, L0_mix_wo, L0_mix_bo)[0]
    x = x + _L0_ffn_ref(_layernorm(x, axis=-1)[None], L0_ffn_Wg, L0_ffn_bg, L0_ffn_W1, L0_ffn_b1, L0_ffn_W2, L0_ffn_b2)[0]
    return x

_drawn_inputs = setup_inputs


def setup_inputs(seed=0):
    import zlib

    import numpy as np

    out = dict(_drawn_inputs(seed))
    spreads = {'L0_gnn_b1l': (0.0, 0.1),
     'L0_gnn_b2l': (0.0, 0.1),
     'L0_mix_bq': (0.0, 0.8),
     'L0_mix_bk': (0.0, 0.8),
     'L0_mix_bv': (0.0, 0.1),
     'L0_mix_bo': (0.0, 0.1),
     'L0_ffn_bg': (0.0, 0.1),
     'L0_ffn_b1': (0.0, 0.398),
     'L0_ffn_b2': (0.0, 0.1)}
    factors = {'L0_mix_wq': 8.0, 'L0_mix_wk': 6.257, 'L0_mix_wv': 3.311}
    for name, (base, spread) in spreads.items():
        noise = np.random.default_rng([zlib.crc32(name.encode()), seed]).standard_normal(out[name].shape)
        drawn = base * np.exp(spread * noise) if base else spread * noise
        out[name] = jnp.asarray(drawn.astype(out[name].dtype))
    for name, factor in factors.items():
        out[name] = (out[name] * factor).astype(out[name].dtype)
    return out
```

```python
import concourse.bass as bass
import numpy as np
from concourse import mybir
from contextlib import ExitStack

P = 128
N_NODES = 3125
D = 256
KD = D // P
HID = 512
KH = HID // P
NT = -(-N_NODES // P)
NP = NT * P
LAST = N_NODES - (NT - 1) * P
E_ALL = 53125
NC = -(-E_ALL // P)
ITEMS = NC + NT - 1
GBUF = 32
STAGE = 16
LN_G = 5
HG = 400
NHG = NP // HG
HEADS = 8
DH = D // HEADS
EXP = 8
TOP = 2
FF = 1024
KF = FF // P
NBLK = (TOP * N_NODES + EXP * (P - 1)) // P
NBLK_PAD = NBLK + 1
BW = FF + D
BC = EXP * BW // P
LN_EPS = 1e-5
NORM_EPS = 1e-6
BIG = 3.0e38

S1_ITEMS, S2_ITEMS, S3_ITEMS = 4, 6, 4
S3_STEPS = NHG * KH
S2_BASE = NT * S1_ITEMS
S3_BASE = S2_BASE + NT * S2_ITEMS
S4_BASE = S3_BASE + S3_STEPS * S3_ITEMS
R_ITEMS = 4
R_BASE = NT * R_ITEMS
assert NC % GBUF == 0 and NT % LN_G == 0 and NP % HG == 0
assert (ITEMS - S4_BASE) % 2 == 0 and (ITEMS - R_BASE) % 2 == 0
assert GBUF > STAGE


def program(nc, x_in_d, src_d, dst_d, wq_d, wkv_d, wo_d, w1l_d, w1r_d, w2l_d, w2r_d,
            rows_d, cols_d, ffw1_d, ffw2_d, ffb_d, wg_d, out_d):
    f32, bf16, i32 = mybir.dt.float32, mybir.dt.bfloat16, mybir.dt.int32
    ALU = mybir.AluOpType
    ACT = mybir.ActivationFunctionType
    AX = mybir.AxisListType
    ds = bass.ds

    xn_d = nc.dram_tensor("xn_rows", (NP, D), f32).ap()
    z_d = nc.dram_tensor("z_rows", (NP, D), f32).ap()
    xs_d = nc.dram_tensor("sorted_tokens", (NBLK_PAD * P, D), f32).ap()
    ys_d = nc.dram_tensor("sorted_outputs", (NBLK * P, D), f32).ap()
    bp_d = nc.dram_tensor("bias_parts", (3, EXP * BW), bf16).ap()

    with ExitStack() as ctx:
        def sb(name, shape, dt=f32):
            return ctx.enter_context(nc.sbuf_tensor(name, shape, dt))

        def ps(name, width):
            return ctx.enter_context(nc.psum_tensor(name, [P, width], f32))

        def sem(name):
            return ctx.enter_context(nc.semaphore(name))

        res = sb("res", [P, NT, D])
        ring = sb("ring", [P, GBUF * D])
        gbuf = ring[:, :].rearrange("p (s d) -> p s d", d=D)
        x2n = ring[:, 0:NT * D].rearrange("p (t d) -> p t d", d=D)

        W1W = EXP * KD * FF
        W2W = EXP * KF * D
        A_XNT = 0
        A_H = A_XNT + KD * NP
        A_AGG = A_H + KH * NP
        A_W = A_AGG + NT * (D + 1)
        A_TMP = A_W + KD * (D + 2 * D + D) + 2 * KD * HID + 2 * KH * D
        A_END = A_TMP + 8 * D + 2 * 2
        arena = sb("arena", [P, max(A_END, W1W + W2W)])

        def area(at, width):
            return arena[:, at:at + width]
        xnT = area(A_XNT, KD * NP).rearrange("p (k n) -> p k n", k=KD)
        aggT = xnT
        hT = area(A_H, KH * NP).rearrange("p (k n) -> p k n", k=KH)
        qT = area(A_H, KD * NP).rearrange("p (k n) -> p k n", k=KD)
        xn = area(A_H + KD * NP, NT * D).rearrange("p (t d) -> p t d", d=D)
        agg = area(A_AGG, NT * (D + 1)).rearrange("p (t d) -> p t d", d=D + 1)
        at = A_W
        wq = area(at, KD * D).rearrange("p (k n) -> p k n", k=KD); at += KD * D
        wkv = area(at, KD * 2 * D).rearrange("p (k n) -> p k n", k=KD); at += KD * 2 * D
        wo = area(at, KD * D).rearrange("p (k n) -> p k n", k=KD); at += KD * D
        w1l = area(at, KD * HID).rearrange("p (k n) -> p k n", k=KD); at += KD * HID
        w1r = area(at, KD * HID).rearrange("p (k n) -> p k n", k=KD); at += KD * HID
        w2l = area(at, KH * D).rearrange("p (k n) -> p k n", k=KH); at += KH * D
        w2r = area(at, KH * D).rearrange("p (k n) -> p k n", k=KH); at += KH * D
        assert at == A_TMP
        exp_k = area(at, D); at += D
        relu_k = area(at, D); at += D
        feat_k = area(at, D); at += D
        val = area(at, 2 * (P + 1)).rearrange("p (h d) -> p h d", h=2); at += 2 * (P + 1)
        exp_q = area(at, D); at += D
        relu_q = area(at, D); at += D
        zrow = area(at, 2 * D).rearrange("p (s d) -> p s d", s=2); at += 2 * D
        assert at <= A_END
        zeros = zrow[:, 0, :]
        bf_part = zrow[:, 1, 0:3 * BC // 2].bitcast(bf16).rearrange("p (k c) -> p k c", k=3)
        at = A_H
        it_all = area(at, ITEMS); at += ITEMS
        cmp_ = area(at, ITEMS); at += ITEMS
        dst_i = area(at, NC).bitcast(i32); at += NC
        dlast_i = area(at, NC).bitcast(i32); at += NC
        bf_full = area(at, BC); at += BC
        bf_left = area(at, BC); at += BC
        assert at <= A_H + KD * NP
        kv_m = area(A_W, 2 * P).rearrange("p (h d) -> p h d", h=2)
        ks_m = area(A_W + 2 * P, 2 * P).rearrange("p (h d) -> p h d", h=2)
        x2T = area(A_TMP + 6 * D + 4, 2 * D).rearrange("p (s d) -> p s d", s=2)
        assert A_TMP + 6 * D + 4 >= W1W + W2W
        pre = area(A_TMP, 2 * HG).rearrange("p (s n) -> p s n", s=2)
        ffw1 = area(0, W1W).rearrange("p (e k n) -> p e k n", e=EXP, k=KD)
        ffw2 = area(W1W, W2W).rearrange("p (e k n) -> p e k n", e=EXP, k=KF)

        m = 0
        xt = ring[:, m:m + 2 * D].rearrange("p (s d) -> p s d", s=2); m += 2 * D
        xT = ring[:, m:m + 2 * D].rearrange("p (s d) -> p s d", s=2); m += 2 * D
        hs = ring[:, m:m + 2 * FF].rearrange("p (s d) -> p s d", s=2); m += 2 * FF
        hsT = ring[:, m:m + 2 * FF].rearrange("p (s d) -> p s d", s=2); m += 2 * FF
        yt = ring[:, m:m + 2 * D].rearrange("p (s d) -> p s d", s=2); m += 2 * D
        b1_p = ring[0:3, m:m + FF].bitcast(bf16).rearrange("p (s d) -> p s d", s=2); m += FF
        b2_p = ring[0:3, m:m + EXP * D // 2].bitcast(bf16); m += EXP * D // 2
        assert m <= GBUF * D
        NY = 8
        yg = ring[:, 0:NY * D].rearrange("p (s d) -> p s d", d=D)

        src = sb("src", [P, NC], i32)
        stage = sb("stage", [P, 2, STAGE], i32)
        dst = sb("dst", [P, NC])
        tab_c = sb("tab_c", [1, ITEMS], i32)
        tab_t = sb("tab_t", [1, ITEMS], i32)
        tab_n = sb("tab_n", [1, NC], i32)
        tab_e = sb("tab_e", [1, NBLK_PAD], i32)
        ident = sb("ident", [P, P])
        tri = sb("tri", [P, P])
        ones = sb("ones", [P, P])
        hmask = sb("hmask", [P, P])
        iota = sb("iota", [P, P])
        neg_t = sb("neg_t", [P, NT])
        onehot = sb("onehot", [P, 2, P])
        rows = sb("rows", [1, 2 * D + 2 * D + EXP])
        bkv_row = rows[0:1, 0:2 * D]
        bo_row, b2_row = rows[0:1, 2 * D:3 * D], rows[0:1, 3 * D:4 * D]
        bg_row = rows[0:1, 4 * D:4 * D + EXP]
        cols = sb("cols", [P, KD + KH])
        ones_b = sb("ones_b", [3, P], bf16)
        wg = sb("wg", [P, KD, EXP])
        st = sb("st", [P, NT, 6])
        mv = sb("mv", [P, NT, 2])
        rstd = sb("rstd", [P, NT])
        rcnt = sb("rcnt", [P, NT])
        BT = NT - 1
        thr = sb("thr", [P, 4])
        R8 = NT * EXP
        at = NT * D

        def routing(*shape):
            nonlocal at
            n = int(np.prod(shape))
            a = ring[:, at:at + n]
            at += n
            return a
        lg = routing(R8).rearrange("p (t e) -> p t e", e=EXP)
        oh1 = routing(R8).rearrange("p (t e) -> p t e", e=EXP)
        oh2 = routing(R8).rearrange("p (t e) -> p t e", e=EXP)
        rt = routing(4 * R8).rearrange("p (k n) -> p k n", k=4)
        valid = routing(R8).rearrange("p (t e) -> p t e", e=EXP)
        assert at <= GBUF * D
        rev8 = sb("rev8", [P, EXP])
        blk = sb("blk", [1, NBLK_PAD])
        at = W1W + W2W

        def small(*shape):
            nonlocal at
            n = int(np.prod(shape))
            a = arena[:, at:at + n]
            at += n
            return a
        m12 = small(4 * NT).rearrange("p (k t) -> p k t", k=4)
        wts = small(4 * NT).rearrange("p (k t) -> p k t", k=4)
        pos = small(2 * NT).bitcast(i32).rearrange("p (k t) -> p k t", k=2)
        nb = small(4 * EXP).rearrange("p (k e) -> p k e", k=4)
        nb_i = small(2 * EXP).bitcast(i32).rearrange("p (k e) -> p k e", k=2)
        assert at <= A_TMP + 6 * D + 4

        bankH = [ps("bankH0", 2 * 512), ps("bankH1", 2 * 512)]
        bankT = ps("bankT", 2 * 512)
        bankX, bankY = ps("bankX", 512), ps("bankY", 512)
        pA, pB = bankH[0][:, 0:512], bankH[0][:, 512:1024]
        pC, pD = bankH[1][:, 0:512], bankH[1][:, 512:1024]
        pE, pF = bankT[:, 0:512], bankT[:, 512:1024]
        p_item = [bankX[:, :], bankY[:, :]]

        x_loaded = [sem(f"x_loaded{g}") for g in range(NT // LN_G)]
        x_zeroed = sem("x_zeroed")
        x_ready = sem("x_ready")
        idx_loaded = sem("idx_loaded")
        dst_loaded = sem("dst_loaded")
        w_loaded = sem("w_loaded")
        xn_stored = sem("xn_stored")
        const_ready = sem("const_ready")
        pool_step = sem("pool_step")
        ln_var, ln_root = sem("ln_var"), sem("ln_root")
        ln_stats, ln_aggr, ln_rstd, xn_ready = sem("ln_stats"), sem("ln_aggr"), sem("ln_rstd"), sem("xn_ready")
        xn_turned, xnT_ready = sem("xn_turned"), sem("xnT_ready")
        thr_ready, tab_cmp, tab_sum, tab_step, tab_ready = (sem("thr_ready"), sem("tab_cmp"), sem("tab_sum"),
                                                           sem("tab_step"), sem("tab_ready"))
        agg_zeroed = sem("agg_zeroed")
        gathered = [sem(f"gathered{s}") for s in range(GBUF)]
        staged = sem("staged")
        arrived = sem("arrived")
        onehot_ready = sem("onehot_ready")
        item_done = sem("item_done")
        item_added = sem("item_added")
        kv_done, q_done, kvq_act, feat_ready = sem("kv_done"), sem("q_done"), sem("kvq_act"), sem("feat_ready")
        ktv_done, ktv_read = sem("ktv_done"), sem("ktv_read")
        ctx_done, att_ready, proj_done, proj_added = (sem("ctx_done"), sem("att_ready"), sem("proj_done"),
                                                      sem("proj_added"))
        hpre_done, hpre_read = sem("hpre_done"), sem("hpre_read")
        cnt_step, agg_scaled, agg_turned, aggT_ready = (sem("cnt_step"), sem("agg_scaled"), sem("agg_turned"),
                                                        sem("aggT_ready"))
        h_done, h_sum, h_ready = sem("h_done"), sem("h_sum"), sem("h_ready")
        z_done, z_copied = sem("z_done"), sem("z_copied")
        z_out = [sem("z_out0"), sem("z_out1")]
        r_done, r_added = sem("r_done"), sem("r_added")
        bias_split, bias_out = sem("bias_split"), sem("bias_out")
        zeros_ready, xs_zeroed = sem("zeros_ready"), sem("xs_zeroed")
        ffw_loaded = sem("ffw_loaded")
        b2_loaded = sem("b2_loaded")
        ln2_step, x2n_ready, x2_turned, x2T_ready = (sem("ln2_step"), sem("x2n_ready"), sem("x2_turned"),
                                                     sem("x2T_ready"))
        logit_done = sem("logit_done")
        route, route_act, route_pe = sem("route"), sem("route_act"), sem("route_pe")
        tokens_placed = sem("tokens_placed")
        xt_loaded = [sem("xt_loaded0"), sem("xt_loaded1")]
        bp_loaded = [sem("bp_loaded0"), sem("bp_loaded1")]
        xt_turned, xT_ready = sem("xt_turned"), sem("xT_ready")
        up_done, act_done, hs_turned, hsT_ready = sem("up_done"), sem("act_done"), sem("hs_turned"), sem("hsT_ready")
        down_done, y_copied = sem("down_done"), sem("y_copied")
        y_out = [sem("y_out0"), sem("y_out1")]
        y_gathered = [sem(f"y_gathered{s}") for s in range(NY)]
        mixed = sem("mixed")
        out_stored = sem("out_stored")
        passed, passed_sp, passed_dve = sem("passed"), sem("passed_sp"), sem("passed_dve")

        N_CONST = 7
        N_W = 12
        block = ctx.enter_context(nc.Block())

        @block.sync
        def _(sp):
            for g in range(NT // LN_G):
                t0, t1 = g * LN_G, min((g + 1) * LN_G, NT - 1)
                sp.dma_start(res[:, t0:t1, :],
                             x_in_d[t0 * P:t1 * P, :].rearrange("(t p) d -> p t d", p=P)).then_inc(x_loaded[g], 16)
            sp.wait_ge(x_zeroed, 1)
            sp.dma_start(res[0:LAST, NT - 1, :], x_in_d[(NT - 1) * P:N_NODES, :]).then_inc(x_loaded[-1], 16)
            sp.dma_start(dst_i[:, :], dst_d).then_inc(dst_loaded, 16)
            sp.dma_start(dlast_i[0:BT, :], dst_d[P - 1:P, :].to_broadcast([BT, NC])).then_inc(dst_loaded, 16)
            sp.dma_start(src[:, :], src_d).then_inc(idx_loaded, 16)
            sp.dma_start(wkv[:, :, :], wkv_d.rearrange("(k p) n -> p k n", p=P)).then_inc(w_loaded, 16)
            sp.dma_start(wq[:, :, :], wq_d.rearrange("(k p) n -> p k n", p=P)).then_inc(w_loaded, 16)
            sp.dma_start(wo[:, :, :], wo_d.rearrange("(k p) n -> p k n", p=P)).then_inc(w_loaded, 16)
            sp.dma_start(w1l[:, :, :], w1l_d.rearrange("(k p) n -> p k n", p=P)).then_inc(w_loaded, 16)
            sp.dma_start(w1r[:, :, :], w1r_d.rearrange("(k p) n -> p k n", p=P)).then_inc(w_loaded, 16)
            sp.dma_start(w2l[:, :, :], w2l_d.rearrange("(k p) n -> p k n", p=P)).then_inc(w_loaded, 16)
            sp.dma_start(w2r[:, :, :], w2r_d.rearrange("(k p) n -> p k n", p=P)).then_inc(w_loaded, 16)
            sp.dma_start(rows[:, :], rows_d).then_inc(w_loaded, 16)
            sp.dma_start(cols[:, :], cols_d).then_inc(w_loaded, 16)
            sp.dma_start(wg[:, :, :], wg_d.rearrange("(k p) n -> p k n", p=P)).then_inc(w_loaded, 16)
            sp.dma_start(bf_full[:, :], ffb_d.rearrange("(p c) -> p c", p=P)).then_inc(w_loaded, 16)
            for g in range(NT // LN_G):
                sp.wait_ge(x_loaded[g], 32 if g == NT // LN_G - 1 else 16)
                sp.sem_inc(x_ready, 1)
            for g in range(NT // LN_G):
                sp.wait_ge(xn_ready, LN_G * (g + 1))
                sp.dma_start(xn_d[g * LN_G * P:(g + 1) * LN_G * P, :].rearrange("(t p) d -> p t d", p=P),
                             xn[:, g * LN_G:(g + 1) * LN_G, :]).then_inc(xn_stored, 16)

            sp.wait_ge(bias_split, 5)
            for k in range(3):
                sp.dma_start(bp_d[k, :].rearrange("(p c) -> p c", p=P), bf_part[:, k, :]).then_inc(bias_out, 16)
            sp.wait_ge(zeros_ready, 1)
            for b in range(NBLK_PAD):
                sp.dma_start(xs_d[b * P:(b + 1) * P, :], zeros).then_inc(xs_zeroed, 16)

            sp.sem_inc(arrived, GBUF)
            with sp.Fori(0, NC // GBUF) as r:
                for s in range(GBUF):
                    sp.wait_ge(gathered[s], r * 16 + 16)
                    sp.sem_inc(arrived, 1)
            with sp.Fori(0, NT // 2) as r:
                for s in range(2):
                    sp.wait_ge(z_copied, r * 2 + s + 3)
                    sp.dma_start(z_d[ds((r * 2 + s) * P, P), :], zrow[:, s, :]).then_inc(z_out[s], 16)
            sp.wait_ge(z_copied, NT + 2)
            sp.dma_start(z_d[(NT - 1) * P:NT * P, :], zrow[:, 0, :]).then_inc(z_out[0], 16)

            with sp.Fori(0, NC // GBUF) as r:
                for s in range(GBUF):
                    sp.wait_ge(gathered[s], r * 16 + (NC // GBUF + 1) * 16)
                    sp.sem_inc(arrived, 1)

            sp.wait_ge(tokens_placed, 2 * NT * 16)
            sp.wait_ge(route, ROUTE_DONE)
            sp.wait_ge(bias_out, 48)
            sp.dma_start(b2_p[:, :], bp_d[:, EXP * FF:EXP * BW]).then_inc(b2_loaded, 16)

            def load_block(b, s):
                sp.dma_start(xt[:, s, :], xs_d[ds(b * P, P), :]).then_inc(xt_loaded[s], 16)
                e = sp.value_load(tab_e[0:1, ds(b, 1)], min_val=0, max_val=EXP - 1)
                sp.dma_start(b1_p[:, s, :], bp_d[:, ds(e * FF, FF)]).then_inc(bp_loaded[s], 16)
            for b in range(2):
                load_block(b, b)
            with sp.Fori(1, NBLK // 2) as r:
                for s in range(2):
                    sp.wait_ge(xt_turned, r * 2 + s - 1)
                    sp.sem_inc(passed_sp, 1)
                    sp.wait_ge(up_done, r * 2 + s + 1)
                    sp.sem_inc(passed_sp, 1)
                    load_block(r * 2 + s, s)
            sp.wait_ge(xt_turned, NBLK - 1)
            sp.dma_start(xt[:, 0, :], xs_d[NBLK * P:NBLK_PAD * P, :]).then_inc(xt_loaded[0], 16)

            for t in range(NT - 1):
                if t % LN_G == LN_G - 1 or t == NT - 2:
                    t0 = t - t % LN_G
                    sp.wait_ge(mixed, 2 * (t + 1))
                    sp.dma_start(out_d[t0 * P:(t + 1) * P, :].rearrange("(t p) d -> p t d", p=P),
                                 res[:, t0:t + 1, :]).then_inc(out_stored, 16)
            sp.wait_ge(mixed, 2 * NT)
            sp.dma_start(out_d[(NT - 1) * P:N_NODES, :], res[0:LAST, NT - 1, :]).then_inc(out_stored, 16)
            sp.wait_ge(out_stored, 16 * (NT // LN_G + 1))

        @block.gpsimd
        def _(pool):
            g = nc.gpsimd
            g.iota(iota[:, :], [[1, P]], base=0, channel_multiplier=0,
                   allow_small_or_imprecise_dtypes=True).then_inc(const_ready, 1)
            g.iota(neg_t[:, :], [[-P, NT]], base=0, channel_multiplier=0,
                   allow_small_or_imprecise_dtypes=True).then_inc(const_ready, 1)
            g.iota(it_all[:, :], [[1, ITEMS]], base=0, channel_multiplier=0,
                   allow_small_or_imprecise_dtypes=True).then_inc(const_ready, 1)
            g.iota(thr[:, 1:2], [[0, 1]], base=1, channel_multiplier=1,
                   allow_small_or_imprecise_dtypes=True).then_inc(const_ready, 1)
            g.iota(rev8[:, :], [[-1, EXP]], base=EXP, channel_multiplier=0,
                   allow_small_or_imprecise_dtypes=True).then_inc(const_ready, 1)
            g.memset(ident[:, :], 0.0).then_inc(pool_step, 1)
            g.memset(ones[:, :], 1.0).then_inc(pool_step, 1)
            g.memset(tri[:, :], 0.0).then_inc(pool_step, 1)
            g.memset(hmask[:, :], 1.0).then_inc(pool_step, 1)
            g.memset(ones_b[:, :], 1.0).then_inc(const_ready, 1)
            pool.wait_ge(pool_step, 4)
            g.affine_select(out=ident[:, :], in_=ident[:, :], compare_op=ALU.not_equal, fill=1.0, base=0,
                            pattern=[[-1, P]], channel_multiplier=1).then_inc(const_ready, 1)
            g.affine_select(out=tri[:, :], in_=tri[:, :], compare_op=ALU.is_ge, fill=1.0, base=0,
                            pattern=[[-1, P]], channel_multiplier=1).then_inc(pool_step, 1)
            hm = hmask[:, :].rearrange("p (h d) -> p h d", d=DH)
            g.affine_select(out=hm, in_=hm, compare_op=ALU.is_ge, fill=0.0, base=0,
                            pattern=[[-DH, P // DH], [0, DH]], channel_multiplier=1).then_inc(pool_step, 1)
            pool.wait_ge(pool_step, 6)
            g.affine_select(out=hm, in_=hm, compare_op=ALU.is_ge, fill=0.0, base=DH - 1,
                            pattern=[[DH, P // DH], [0, DH]], channel_multiplier=-1).then_inc(const_ready, 1)

            pool.wait_ge(idx_loaded, 16)

            def gather_chunks(table, r, first, stage_no):
                for half in range(GBUF // STAGE):
                    if not first:
                        pool.wait_ge(arrived, stage_no[0] + half * STAGE)
                    g.tensor_copy(stage[:, half, :], src[:, ds(r * GBUF + half * STAGE, STAGE)]).then_inc(staged, 1)
                    pool.wait_ge(staged, stage_no[1] + half)
                    pool.sem_inc(passed, 1)
                    for u in range(STAGE):
                        s = half * STAGE + u
                        if not first:
                            need = pool.value_load(tab_n[0:1, ds((r - 1) * GBUF + s, 1)], min_val=0, max_val=ITEMS)
                            pool.wait_ge(item_done, need + stage_no[2])
                            pool.sem_inc(passed, 1)
                        g.indirect_dma_start(
                            out=gbuf[:, s, :], out_offset=None, in_=table,
                            in_offset=bass.IndirectOffsetOnAxis(ap=stage[:, half, u:u + 1], axis=0),
                        ).then_inc(gathered[s], 16)
            halves = GBUF // STAGE
            pool.wait_ge(xn_stored, 16 * (NT // LN_G))
            gather_chunks(xn_d, 0, True, (0, 1, 0))
            pool.wait_ge(tab_ready, 3)
            with pool.Fori(1, NC // GBUF) as r:
                gather_chunks(xn_d, r, False, (r * GBUF + STAGE, r * halves + 1, 2))
            pool.wait_ge(z_out[0], 16 * (NT // 2 + 1))
            pool.wait_ge(z_out[1], 16 * (NT // 2))
            pool.wait_ge(item_done, ITEMS + 2)
            rounds = NC // GBUF
            gather_chunks(z_d, 0, True, (0, rounds * halves + 1, 0))
            with pool.Fori(1, rounds) as r:
                gather_chunks(z_d, r, False, (r * GBUF + NC + STAGE, r * halves + rounds * halves + 1, ITEMS + 2))

            pool.wait_ge(item_done, 2 * ITEMS + 2)
            g.memset(valid[:, :, :], 1.0).then_inc(pool_step, 1)
            pool.wait_ge(pool_step, 7)
            g.affine_select(out=valid[:, :, :], in_=valid[:, :, :], compare_op=ALU.is_ge, fill=0.0,
                            base=N_NODES - 1, pattern=[[-P, NT], [0, EXP]],
                            channel_multiplier=-1).then_inc(pool_step, 1)
            pool.wait_ge(xs_zeroed, 16 * NBLK_PAD)
            pool.wait_ge(route, ROUTE_POS)
            for t in range(NT):
                rows_here = LAST if t == NT - 1 else P
                for k in range(TOP):
                    g.indirect_dma_start(
                        out=xs_d, out_offset=bass.IndirectOffsetOnAxis(ap=pos[0:rows_here, k, t:t + 1], axis=0),
                        in_=x2n[0:rows_here, t, :], in_offset=None).then_inc(tokens_placed, 16)
            pool.wait_ge(y_out[0], 16 * (NBLK // 2))
            pool.wait_ge(y_out[1], 16 * (NBLK // 2))
            for n in range(TOP * NT):
                t, k = n // TOP, n % TOP
                rows_here = LAST if t == NT - 1 else P
                if n >= NY:
                    pool.wait_ge(mixed, n - NY + 1)
                g.indirect_dma_start(
                    out=yg[0:rows_here, n % NY, :], out_offset=None, in_=ys_d,
                    in_offset=bass.IndirectOffsetOnAxis(ap=pos[0:rows_here, k, t:t + 1], axis=0),
                ).then_inc(y_gathered[n % NY], 16)

        @block.vector
        def _(dve):
            v = nc.vector
            v.memset(res[:, NT - 1, :], 0.0).then_inc(x_zeroed, 1)
            v.memset(agg[:, :, :], 0.0).then_inc(agg_zeroed, 1)
            v.memset(val[:, :, P:P + 1], 1.0).then_inc(agg_zeroed, 1)

            def stats(t, m):
                v.bn_stats(st[:, ds(m, 1), :].rearrange("p a d -> p (a d)"),
                           res[:, ds(t, 1), :].rearrange("p a d -> p (a d)")).then_inc(ln_stats, 1)

            def normalize(out, t, m, done):
                v.tensor_scalar(out[:, ds(t, 1), :].rearrange("p a d -> p (a d)"),
                                res[:, ds(t, 1), :].rearrange("p a d -> p (a d)"), mv[:, ds(m, 1), 0:1].rearrange("p a d -> p (a d)"),
                                rstd[:, ds(m, 1)], ALU.subtract, ALU.mult).then_inc(done, 1)
            with dve.Fori(0, NT // LN_G) as gr:
                dve.wait_ge(x_ready, gr + 1)
                for u in range(LN_G):
                    stats(gr * LN_G + u, u)
                dve.wait_ge(ln_stats, gr * LN_G + LN_G)
                dve.sem_inc(passed_dve, 1)
                for u in range(LN_G):
                    v.bn_aggr(mv[:, u, :], st[:, u, :]).then_inc(ln_aggr, 1)
                dve.wait_ge(ln_aggr, gr * LN_G + LN_G)
                five = slice(0, LN_G)
                v.tensor_scalar(rstd[:, five], mv[:, five, 1], LN_EPS, None, ALU.add).then_inc(ln_var, 1)
                dve.wait_ge(ln_root, gr + 1)
                v.reciprocal(rstd[:, five], rstd[:, five]).then_inc(ln_rstd, 1)
                dve.wait_ge(ln_rstd, gr + 1)
                for u in range(LN_G):
                    normalize(xn, gr * LN_G + u, u, xn_ready)

            dve.wait_ge(dst_loaded, 32)
            dve.wait_ge(const_ready, N_CONST + 1)
            v.tensor_copy(dst[:, :], dst_i[:, :]).then_inc(thr_ready, 1)
            v.tensor_scalar(thr[:, 0:1], thr[:, 1:2], float(P), None, ALU.mult).then_inc(thr_ready, 1)
            dve.wait_ge(thr_ready, 2)
            v.tensor_scalar(cmp_[0:BT, 0:NC], dlast_i[0:BT, :], thr[0:BT, 0:1], None, ALU.is_lt).then_inc(thr_ready, 1)
            dve.wait_ge(thr_ready, 3)
            v.tensor_reduce(thr[0:BT, 2:3], cmp_[0:BT, 0:NC], AX.X, ALU.add).then_inc(thr_ready, 1)
            dve.wait_ge(thr_ready, 4)
            v.tensor_tensor(thr[0:BT, 3:4], thr[0:BT, 1:2], thr[0:BT, 2:3], ALU.add).then_inc(thr_ready, 1)
            dve.wait_ge(thr_ready, 5)
            v.tensor_scalar(cmp_[0:BT, :], it_all[0:BT, :], thr[0:BT, 3:4], None, ALU.is_ge).then_inc(tab_cmp, 1)
            dve.wait_ge(tab_sum, 1)
            v.tensor_copy(tab_t[:, :], pE[0:1, 0:ITEMS]).then_inc(tab_ready, 1)
            v.tensor_tensor(tab_c[:, :], it_all[0:1, :], pE[0:1, 0:ITEMS], ALU.subtract).then_inc(tab_ready, 1)
            v.tensor_scalar(cmp_[0:BT, 0:NC], it_all[0:BT, 0:NC], thr[0:BT, 2:3], None, ALU.is_ge).then_inc(tab_cmp, 1)
            dve.wait_ge(tab_sum, 2)
            v.scalar_tensor_tensor(tab_n[:, :], pE[0:1, 0:NC], 1.0, it_all[0:1, 0:NC], ALU.add,
                                   ALU.add).then_inc(tab_ready, 1)
            dve.wait_ge(tab_ready, 3)
            v.memset(zeros, 0.0).then_inc(zeros_ready, 1)
            dve.wait_ge(w_loaded, 16 * N_W_LOADS)
            v.tensor_copy(bf_part[:, 0, :], bf_full[:, :]).then_inc(bias_split, 1)
            dve.wait_ge(bias_split, 1)
            v.tensor_tensor(bf_left, bf_full[:, :], bf_part[:, 0, :], ALU.subtract).then_inc(bias_split, 1)
            dve.wait_ge(bias_split, 2)
            v.tensor_copy(bf_part[:, 1, :], bf_left).then_inc(bias_split, 1)
            dve.wait_ge(bias_split, 3)
            v.tensor_tensor(bf_left, bf_left, bf_part[:, 1, :], ALU.subtract).then_inc(bias_split, 1)
            dve.wait_ge(bias_split, 4)
            v.tensor_copy(bf_part[:, 2, :], bf_left).then_inc(bias_split, 1)

            def one_hot(i, s, base):
                c = dve.value_load(tab_c[0:1, ds(i, 1)], min_val=0, max_val=NC - 1)
                t = dve.value_load(tab_t[0:1, ds(i, 1)], min_val=0, max_val=NT - 1)
                dve.wait_ge(item_done, i + base + 1)
                v.tensor_scalar(onehot[:, s, :], iota[:, :], dst[:, ds(c, 1)], neg_t[:, ds(t, 1)],
                                ALU.subtract, ALU.is_equal).then_inc(onehot_ready, 1)

            def add_item1(i, s):
                t = dve.value_load(tab_t[0:1, ds(i, 1)], min_val=0, max_val=NT - 1)
                dve.wait_ge(item_done, i + 3)
                dve.wait_ge(item_added, i + 2)
                a = agg[:, ds(t, 1), :].rearrange("p a d -> p (a d)")
                v.tensor_tensor(a, p_item[s][:, 0:D + 1], a, ALU.add).then_inc(item_added, 1)

            def add_item2(i, s):
                t = dve.value_load(tab_t[0:1, ds(i, 1)], min_val=0, max_val=NT - 1)
                dve.wait_ge(item_done, i + ITEMS + 3)
                dve.wait_ge(item_added, i + ITEMS + 2)
                a = res[:, ds(t, 1), :].rearrange("p a d -> p (a d)")
                v.scalar_tensor_tensor(a, p_item[s][:, 0:D], rcnt[:, ds(t, 1)], a, ALU.mult,
                                       ALU.add).then_inc(item_added, 1)

            def items1(base, n):
                for u in range(n):
                    one_hot(base + u, u % 2, 0)
                    add_item1(base + u, u % 2)

            def items2(base, n):
                for u in range(n):
                    one_hot(base + u, u % 2, ITEMS)
                    add_item2(base + u, u % 2)

            dve.wait_ge(agg_zeroed, 2)
            dve.sem_inc(feat_ready, 2)
            with dve.Fori(0, NT) as t:
                items1(t * S1_ITEMS, 2)
                dve.wait_ge(kvq_act, t * 2 + 1)
                v.scalar_tensor_tensor(feat_k, exp_k, 1.0, relu_k, ALU.min, ALU.add).then_inc(feat_ready, 1)
                dve.wait_ge(kvq_act, t * 2 + 2)
                v.scalar_tensor_tensor(qT[:, :, ds(t * P, P)], exp_q.rearrange("p (k n) -> p k n", k=KD), 1.0,
                                       relu_q.rearrange("p (k n) -> p k n", k=KD), ALU.min,
                                       ALU.add).then_inc(feat_ready, 1)
                for u in range(2, S1_ITEMS):
                    one_hot(t * S1_ITEMS + u, u % 2, 0)
                    add_item1(t * S1_ITEMS + u, u % 2)
            dve.wait_ge(ktv_done, NT + 1)
            for h, p_kv in enumerate((pC, pD)):
                v.tensor_tensor(kv_m[:, h, :], p_kv[:, 0:P], hmask[:, :], ALU.mult).then_inc(ktv_read, 1)
                v.tensor_scalar(ks_m[:, h, :], hmask[:, :], p_kv[:, P:P + 1], None, ALU.mult).then_inc(ktv_read, 1)
            with dve.Fori(0, NT) as t:
                dve.wait_ge(ctx_done, t + 1)
                v.tensor_scalar(exp_q, pB[:, 0:D], NORM_EPS, None, ALU.add).then_inc(att_ready, 1)
                dve.wait_ge(att_ready, t * 3 + 1)
                v.reciprocal(relu_q, exp_q).then_inc(att_ready, 1)
                dve.wait_ge(att_ready, t * 3 + 2)
                v.tensor_tensor(qT[:, :, ds(t * P, P)], pA[:, 0:D].rearrange("p (k n) -> p k n", k=KD),
                                relu_q.rearrange("p (k n) -> p k n", k=KD), ALU.mult).then_inc(att_ready, 1)
                items1(t * S2_ITEMS + S2_BASE, S2_ITEMS)
                dve.wait_ge(proj_done, t + 1)
                r = res[:, ds(t, 1), :].rearrange("p a d -> p (a d)")
                v.tensor_tensor(r, pE[:, 0:D], r, ALU.add).then_inc(proj_added, 1)
            with dve.Fori(0, S3_STEPS) as q:
                items1(q * S3_ITEMS + S3_BASE, S3_ITEMS)
            with dve.Fori(0, (ITEMS - S4_BASE) // 2) as q:
                items1(q * 2 + S4_BASE, 2)

            dve.wait_ge(item_added, ITEMS + 2)
            v.tensor_scalar(rcnt[:, :], agg[:, :, D], 1.0, None, ALU.max).then_inc(cnt_step, 1)
            dve.wait_ge(cnt_step, 1)
            v.reciprocal(rcnt[:, :], rcnt[:, :]).then_inc(cnt_step, 1)
            dve.wait_ge(cnt_step, 2)
            with dve.Fori(0, NT) as t:
                a = agg[:, ds(t, 1), 0:D].rearrange("p a d -> p (a d)")
                v.tensor_scalar(a, a, rcnt[:, ds(t, 1)], None, ALU.mult).then_inc(agg_scaled, 1)
            with dve.Fori(0, S3_STEPS // 2) as q:
                for s in range(2):
                    n0 = (q * 2 + s) // KH
                    k = (q * 2 + s) % KH
                    dve.wait_ge(h_done, q * 2 + s + 1)
                    dve.wait_ge(h_ready, q * 2 + s + 1)
                    v.tensor_tensor(pre[:, s, :].rearrange("p (a n) -> p a n", a=1), (pA, pB)[s][:, 0:HG].rearrange("p (a n) -> p a n", a=1),
                                    hT[:, ds(k, 1), ds(n0 * HG, HG)], ALU.add).then_inc(h_sum, 1)

            with dve.Fori(0, NT) as t:
                items2(t * R_ITEMS, R_ITEMS)
                dve.wait_ge(r_done, t + 1)
                dve.wait_ge(item_added, t * R_ITEMS + R_ITEMS + ITEMS + 2)
                r = res[:, ds(t, 1), :].rearrange("p a d -> p (a d)")
                v.tensor_tensor(r, pE[:, 0:D], r, ALU.add).then_inc(r_added, 1)
                dve.wait_ge(r_added, t + 1)
            with dve.Fori(0, (ITEMS - R_BASE) // 2) as q:
                items2(q * 2 + R_BASE, 2)

            dve.wait_ge(item_added, 2 * ITEMS + 2)
            with dve.Fori(0, NT) as t:
                stats(t, t)
            dve.wait_ge(ln_stats, 2 * NT)
            for t in range(NT):
                v.bn_aggr(mv[:, t, :], st[:, t, :]).then_inc(ln_aggr, 1)
            dve.wait_ge(ln_aggr, 2 * NT)
            v.tensor_scalar(rstd[:, :], mv[:, :, 1], LN_EPS, None, ALU.add).then_inc(ln_var, 1)
            dve.wait_ge(ln_root, NT // LN_G + 1)
            v.reciprocal(rstd[:, :], rstd[:, :]).then_inc(ln_rstd, 1)
            dve.wait_ge(ln_rstd, NT // LN_G + 1)
            with dve.Fori(0, NT) as t:
                normalize(x2n, t, t, x2n_ready)

            n_route = [0]

            def step(ins):
                n_route[0] += 1
                ins.then_inc(route, 1)
                dve.wait_ge(route, n_route[0])

            def b8(a):
                return a.unsqueeze(2).to_broadcast([P, NT, EXP])

            def flat(a):
                return a.rearrange("p t e -> p (t e)")
            dve.wait_ge(logit_done, NT + 2)
            tmp = [rt[:, k, :].rearrange("p (t e) -> p t e", e=EXP) for k in range(4)]
            step(v.tensor_copy(lg, pF[:, 0:R8].rearrange("p (t e) -> p t e", e=EXP)))
            for k, oh in enumerate((oh1, oh2)):
                L = (lg, tmp[3])[k]
                step(v.tensor_reduce(m12[:, k, :], L, AX.X, ALU.max))
                step(v.tensor_tensor(tmp[0], L, b8(m12[:, k, :]), ALU.is_equal))
                step(v.tensor_tensor(tmp[1], tmp[0], rev8[:, :].unsqueeze(1).to_broadcast([P, NT, EXP]), ALU.mult))
                step(v.tensor_reduce(m12[:, 2 + k, :], tmp[1], AX.X, ALU.max))
                step(v.tensor_tensor(oh[:, :, :], tmp[1], b8(m12[:, 2 + k, :]), ALU.is_equal))
                if k == 0:
                    step(v.scalar_tensor_tensor(flat(tmp[3]), flat(oh1[:, :, :]), -BIG, flat(L), ALU.mult,
                                                ALU.add))
            step(v.tensor_tensor(wts[:, 0, :], m12[:, 1, :], m12[:, 0, :], ALU.subtract))
            EXP_IN = n_route[0]
            dve.wait_ge(pool_step, 8)
            step(v.tensor_tensor(tmp[0], oh1[:, :, :], oh2[:, :, :], ALU.add))
            step(v.tensor_tensor(tmp[0], tmp[0], valid[:, :, :], ALU.mult))
            MEMBERS = n_route[0]
            dve.wait_ge(route_act, 1)
            step(v.tensor_scalar(wts[:, 3, :], wts[:, 2, :], 1.0, None, ALU.add))
            step(v.reciprocal(wts[:, 0, :], wts[:, 3, :]))
            step(v.tensor_tensor(wts[:, 1, :], wts[:, 2, :], wts[:, 0, :], ALU.mult))
            dve.wait_ge(route_pe, 2)
            tot = rt[:, 1, :].rearrange("p (e t) -> p e t", e=EXP)
            cum = rt[:, 2, :].rearrange("p (e t) -> p e t", e=EXP)
            step(v.tensor_copy(tot, pB[:, 0:R8].rearrange("p (t e) -> p e t", e=EXP)))
            for e in range(EXP):
                step(v.tensor_tensor_scan(cum[:, e, :], ones[:, 0:NT], tot[:, e, :], 0.0, ALU.mult, ALU.add))
            step(v.tensor_scalar(nb_i[:, 0, :], cum[:, :, NT - 1], float(P - 1), None, ALU.add))
            step(v.tensor_scalar(nb_i[:, 1, :], nb_i[:, 0, :], 7, None, ALU.arith_shift_right))
            step(v.tensor_copy(nb[:, 0, :], nb_i[:, 1, :]))
            step(v.tensor_tensor_scan(nb[:, 1, :], ones[:, 0:EXP], nb[:, 0, :], 0.0, ALU.mult, ALU.add))
            step(v.tensor_tensor(nb[:, 2, :], nb[:, 1, :], nb[:, 0, :], ALU.subtract))
            step(v.tensor_scalar(nb[:, 3, :], nb[:, 2, :], float(P), None, ALU.mult))
            step(v.tensor_tensor(cum, cum, tot, ALU.subtract))
            step(v.tensor_tensor(tmp[3], pA[:, 0:R8].rearrange("p (t e) -> p t e", e=EXP),
                                 cum.rearrange("p e t -> p t e"), ALU.add))
            step(v.tensor_tensor(tmp[3], tmp[3], nb[:, 3, :].unsqueeze(1).to_broadcast([P, NT, EXP]), ALU.add))
            for k, oh in enumerate((oh1, oh2)):
                step(v.tensor_tensor(tmp[1], tmp[3], oh[:, :, :], ALU.mult))
                step(v.tensor_reduce(m12[:, k, :], tmp[1], AX.X, ALU.add))
                step(v.tensor_copy(pos[:, k, :], m12[:, k, :]))
            assert n_route[0] == ROUTE_POS and EXP_IN == ROUTE_EXP and MEMBERS == ROUTE_MEMBERS
            step(v.memset(blk[:, :], 0.0))
            for e in range(EXP - 1):
                step(v.scalar_tensor_tensor(blk[:, :], iota[0:1, 0:NBLK_PAD], nb[0:1, 1, e:e + 1], blk[:, :], ALU.is_ge, ALU.add))
            step(v.tensor_copy(tab_e[:, :], blk[:, :]))
            assert n_route[0] == ROUTE_DONE

            dve.wait_ge(tokens_placed, 2 * NT * 16)

            def copy_xT(b, s):
                dve.wait_ge(xt_turned, b + 1)
                dve.wait_ge(up_done, b + 1)
                v.tensor_copy(xT[:, s, :], bankX[:, 0:D]).then_inc(xT_ready, 1)

            def copy_hsT(b, s):
                dve.wait_ge(hs_turned, b + 1)
                dve.wait_ge(down_done, b + 1)
                v.tensor_copy(hsT[:, s, :], bankT[:, :]).then_inc(hsT_ready, 1)
            copy_xT(0, 0)
            copy_xT(1, 1)
            with dve.Fori(0, NBLK // 2 - 1) as r:
                for s in range(2):
                    copy_xT(r * 2 + s + 2, s)
                    copy_hsT(r * 2 + s, s)
            copy_xT(NBLK, 0)
            copy_hsT(NBLK - 2, 0)
            copy_hsT(NBLK - 1, 1)
            for n in range(TOP * NT):
                t, k = n // TOP, n % TOP
                dve.wait_ge(y_gathered[n % NY], 16 * (n // NY + 1))
                if k:
                    dve.wait_ge(mixed, n)
                rows_here = LAST if t == NT - 1 else P
                v.scalar_tensor_tensor(res[0:rows_here, t, :], yg[0:rows_here, n % NY, :],
                                       wts[0:rows_here, k, t:t + 1], res[0:rows_here, t, :], ALU.mult,
                                       ALU.add).then_inc(mixed, 1)

        @block.scalar
        def _(act):
            a = nc.scalar
            act.sem_inc(xnT_ready, LN_G)
            with act.Fori(0, NT // LN_G) as gr:
                five = slice(0, LN_G)
                act.wait_ge(ln_var, gr + 1)
                a.activation(rstd[:, five], rstd[:, five], ACT.Sqrt).then_inc(ln_root, 1)
                for u, bank in enumerate((pA, pB, pC, pD, pE)):
                    act.wait_ge(xn_turned, gr * LN_G + u + 1)
                    a.activation(xnT[:, :, ds((gr * LN_G + u) * P, P)], bank[:, 0:D].rearrange("p (k n) -> p k n", k=KD),
                                 ACT.Copy).then_inc(xnT_ready, 1)
            act.wait_ge(w_loaded, 16 * N_W_LOADS)
            act.wait_ge(agg_zeroed, 2)
            with act.Fori(0, NT) as t:
                act.wait_ge(kv_done, t + 1)
                act.wait_ge(ktv_done, t + 1)
                act.wait_ge(feat_ready, t * 2 + 2)
                a.activation(exp_k, pA[:, 0:D], ACT.Exp)
                a.activation(relu_k, pA[:, 0:D], ACT.Relu)
                a.activation(val[:, :, 0:P], pA[:, D:2 * D].rearrange("p (h d) -> p h d", h=2),
                             ACT.Copy).then_inc(kvq_act, 1)
                act.wait_ge(q_done, t + 1)
                for k in range(KD):
                    a.activation(exp_q[:, k * P:(k + 1) * P], pB[:, k * P:(k + 1) * P], ACT.Exp, bias=cols[:, k:k + 1])
                    last = a.activation(relu_q[:, k * P:(k + 1) * P], pB[:, k * P:(k + 1) * P], ACT.Relu,
                                        bias=cols[:, k:k + 1])
                last.then_inc(kvq_act, 1)
            act.sem_inc(hpre_read, 2)
            with act.Fori(0, NHG) as gr:
                for k in range(KH):
                    act.wait_ge(hpre_done, gr * KH + k + 1)
                    a.activation(hT[:, k, ds(gr * HG, HG)], (pA, pB)[k % 2][:, 0:HG], ACT.Identity,
                                 bias=cols[:, KD + k:KD + k + 1]).then_inc(hpre_read, 1)
            act.sem_inc(aggT_ready, 4)
            with act.Fori(0, (NT - 1) // 4) as gr:
                for u, bank in enumerate((pA, pB, pC, pD)):
                    act.wait_ge(agg_turned, gr * 4 + u + 1)
                    a.activation(aggT[:, :, ds((gr * 4 + u) * P, P)], bank[:, 0:D].rearrange("p (k n) -> p k n", k=KD),
                                 ACT.Copy).then_inc(aggT_ready, 1)
            act.wait_ge(agg_turned, NT)
            a.activation(aggT[:, :, (NT - 1) * P:NT * P], pA[:, 0:D].rearrange("p (k n) -> p k n", k=KD),
                         ACT.Copy).then_inc(aggT_ready, 1)
            act.sem_inc(h_ready, 2)
            with act.Fori(0, NHG) as gr:
                for k in range(KH):
                    act.wait_ge(h_sum, gr * KH + k + 1)
                    a.activation(hT[:, k, ds(gr * HG, HG)], pre[:, k % 2, :], ACT.Relu).then_inc(h_ready, 1)
            act.sem_inc(z_copied, 2)
            act.wait_ge(xs_zeroed, 16 * NBLK_PAD)
            act.wait_ge(bias_out, 48)
            for s in range(2):
                act.wait_ge(z_done, s + 1)
                a.activation(zrow[:, s, :], (pC, pD)[s][:, 0:D], ACT.Copy).then_inc(z_copied, 1)
            with act.Fori(1, NT // 2) as r:
                for s in range(2):
                    act.wait_ge(z_done, r * 2 + s + 1)
                    act.wait_ge(z_out[s], r * 16)
                    a.activation(zrow[:, s, :], (pC, pD)[s][:, 0:D], ACT.Copy).then_inc(z_copied, 1)
            act.wait_ge(z_done, NT)
            act.wait_ge(z_out[0], 16 * (NT // 2))
            a.activation(zrow[:, 0, :], pC[:, 0:D], ACT.Copy).then_inc(z_copied, 1)
            act.wait_ge(r_done, NT)
            act.wait_ge(z_out[0], 16 * (NT // 2 + 1))
            act.wait_ge(z_out[1], 16 * (NT // 2))
            for e in range(EXP):
                act.dma_start(ffw1[:, e, :, :], ffw1_d[e].rearrange("(k p) n -> p k n", p=P)).then_inc(ffw_loaded, 16)
                act.dma_start(ffw2[:, e, :, :], ffw2_d[e].rearrange("(k p) n -> p k n", p=P)).then_inc(ffw_loaded, 16)
            act.wait_ge(ln_var, NT // LN_G + 1)
            a.activation(rstd[:, :], rstd[:, :], ACT.Sqrt).then_inc(ln_root, 1)
            act.sem_inc(x2T_ready, 2)
            with act.Fori(0, NT // 2) as r:
                for s in range(2):
                    act.wait_ge(x2_turned, r * 2 + s + 1)
                    act.wait_ge(logit_done, r * 2 + s + 1)
                    a.activation(x2T[:, s, :], (pC, pD)[s][:, 0:D], ACT.Copy).then_inc(x2T_ready, 1)
            act.wait_ge(x2_turned, NT)
            act.wait_ge(logit_done, NT)
            a.activation(x2T[:, 0, :], pC[:, 0:D], ACT.Copy).then_inc(x2T_ready, 1)
            act.wait_ge(route, ROUTE_EXP)
            a.activation(wts[:, 2, :], wts[:, 0, :], ACT.Exp).then_inc(route_act, 1)

            act.wait_ge(tokens_placed, 2 * NT * 16)

            def gelu(b, s):
                act.wait_ge(up_done, b + 3)
                a.activation(hs[:, s, :], bankH[s][:, :], ACT.Gelu).then_inc(act_done, 1)

            def store_y(b, s):
                act.wait_ge(down_done, b + 3)
                a.activation(yt[:, s, :], bankY[:, 0:D], ACT.Copy).then_inc(y_copied, 1)
                act.wait_ge(y_copied, b + 2)
                act.dma_start(ys_d[ds(b * P, P), :], yt[:, s, :]).then_inc(y_out[s], 16)
            act.sem_inc(y_copied, 1)
            for b in range(2):
                gelu(b, b)
            for b in range(2):
                act.wait_ge(hs_turned, b + 1)
                gelu(b + 2, b)
                store_y(b, b)
            with act.Fori(1, NBLK // 2 - 1) as r:
                for s in range(2):
                    act.wait_ge(hs_turned, r * 2 + s + 1)
                    gelu(r * 2 + s + 2, s)
                    act.wait_ge(y_out[s], r * 16)
                    store_y(r * 2 + s, s)
            for s in range(2):
                act.wait_ge(y_out[s], (NBLK // 2 - 1) * 16)
                store_y(NBLK - 2 + s, s)

        @block.tensor
        def _(pe):
            t_ = nc.tensor
            pe.wait_ge(const_ready, N_CONST + 1)
            for gr in range(NT // LN_G):
                for u, bank in enumerate((pA, pB, pC, pD, pE)):
                    pe.wait_ge(xn_ready, gr * LN_G + u + 1)
                    pe.wait_ge(xnT_ready, gr * LN_G + u + 1)
                    for k in range(KD):
                        last = t_.transpose(bank[:, k * P:(k + 1) * P],
                                            xn[:, gr * LN_G + u, k * P:(k + 1) * P], ident[:, :])
                    last.then_inc(xn_turned, 1)
            pe.wait_ge(xnT_ready, NT + LN_G)
            pe.wait_ge(tab_cmp, 1)
            t_.matmul(pE[:, 0:ITEMS], ones[0:BT, :], cmp_[0:BT, :], start=True, stop=True).then_inc(tab_sum, 1)
            pe.wait_ge(tab_cmp, 2)
            pe.wait_ge(tab_ready, 2)
            t_.matmul(pE[:, 0:NC], ones[0:BT, :], cmp_[0:BT, 0:NC], start=True, stop=True).then_inc(tab_sum, 1)
            pe.wait_ge(tab_ready, 3)
            pe.sem_inc(item_done, 2)
            pe.sem_inc(item_added, 2)
            pe.wait_ge(w_loaded, 16 * N_W_LOADS)

            def item(i, s, layer):
                c = pe.value_load(tab_c[0:1, ds(i, 1)], min_val=0, max_val=NC - 1)
                slot = c % GBUF
                pe.wait_ge(arrived, c + (GBUF + 1 + layer * NC))
                pe.wait_ge(onehot_ready, i + 1 + layer * ITEMS)
                pe.wait_ge(item_added, i + 1 + layer * ITEMS)
                g = gbuf[:, ds(slot, 1), :].rearrange("p a d -> p (a d)")
                last = t_.matmul(p_item[s][:, 0:D], onehot[:, s, :], g, start=True, stop=True)
                if layer == 0:
                    last = t_.matmul(p_item[s][:, D:D + 1], onehot[:, s, :], ones[:, 0:1], start=True, stop=True)
                last.then_inc(item_done, 1)

            def items(base, n, layer):
                for u in range(n):
                    item(base + u, u % 2, layer)

            def s1(t, first, last_tile):
                n = LAST if last_tile else P
                nodes = slice(t * P, (t + 1) * P)
                if not first:
                    pe.wait_ge(kvq_act, t * 2)
                for k in range(KD):
                    t_.matmul(pA[:, :], xnT[:, k, nodes], wkv[:, k, :], start=k == 0, stop=False)
                t_.matmul(pA[:, :], ones[0:1, :], bkv_row, start=False, stop=True).then_inc(kv_done, 1)
                for half in range(KD):
                    for k in range(KD):
                        last = t_.matmul(pB[:, half * P:(half + 1) * P], wq[:, k, half * P:(half + 1) * P],
                                         xnT[:, k, nodes], start=k == 0, stop=k == KD - 1)
                last.then_inc(q_done, 1)
                items(t * S1_ITEMS, S1_ITEMS, 0)
                pe.wait_ge(feat_ready, t * 2 + 3)
                for h, p_kv in enumerate((pC, pD)):
                    last = t_.matmul(p_kv[:, 0:P + 1], feat_k[0:n, h * P:(h + 1) * P], val[0:n, h, :],
                                     start=first, stop=last_tile)
                last.then_inc(ktv_done, 1)
            pe.sem_inc(ktv_done, 1)
            s1(0, True, False)
            for t in range(1, NT - 1):
                s1(t, False, False)
            s1(NT - 1, False, True)

            pe.wait_ge(ktv_read, 4)
            pe.wait_ge(feat_ready, 2 * NT + 2)
            pe.sem_inc(proj_added, 1)
            for t in range(NT):
                nodes = slice(t * P, (t + 1) * P)
                pe.wait_ge(proj_added, t + 1)
                for bank, mat in ((pA, kv_m), (pB, ks_m)):
                    for h in range(KD):
                        last = t_.matmul(bank[:, h * P:(h + 1) * P], mat[:, h, :], qT[:, h, nodes],
                                         start=True, stop=True)
                last.then_inc(ctx_done, 1)
                items(t * S2_ITEMS + S2_BASE, S2_ITEMS, 0)
                pe.wait_ge(att_ready, t * 3 + 3)
                for h in range(KD):
                    t_.matmul(pE[:, 0:D], qT[:, h, nodes], wo[:, h, :], start=h == 0, stop=False)
                t_.matmul(pE[:, 0:D], ones[0:1, :], bo_row, start=False, stop=True).then_inc(proj_done, 1)

            pe.wait_ge(proj_added, NT + 1)
            with pe.Fori(0, NHG) as gr:
                for k4 in range(KH):
                    pe.wait_ge(hpre_read, gr * KH + k4 + 1)
                    for k in range(KD):
                        last = t_.matmul((pA, pB)[k4 % 2][:, 0:HG], w1r[:, k, k4 * P:(k4 + 1) * P],
                                         xnT[:, k, ds(gr * HG, HG)], start=k == 0, stop=k == KD - 1)
                    last.then_inc(hpre_done, 1)
                    items((gr * KH + k4) * S3_ITEMS + S3_BASE, S3_ITEMS, 0)
            with pe.Fori(0, (ITEMS - S4_BASE) // 2) as q:
                items(q * 2 + S4_BASE, 2, 0)

            pe.wait_ge(hpre_read, S3_STEPS + 2)
            for gr in range((NT - 1) // 4):
                for u, bank in enumerate((pA, pB, pC, pD)):
                    pe.wait_ge(agg_scaled, gr * 4 + u + 1)
                    pe.wait_ge(aggT_ready, gr * 4 + u + 1)
                    for k in range(KD):
                        last = t_.transpose(bank[:, k * P:(k + 1) * P],
                                            agg[:, gr * 4 + u, k * P:(k + 1) * P], ident[:, :])
                    last.then_inc(agg_turned, 1)
            pe.wait_ge(agg_scaled, NT)
            pe.wait_ge(aggT_ready, NT)
            for k in range(KD):
                last = t_.transpose(pA[:, k * P:(k + 1) * P], agg[:, NT - 1, k * P:(k + 1) * P], ident[:, :])
            last.then_inc(agg_turned, 1)
            pe.wait_ge(aggT_ready, NT + 4)
            with pe.Fori(0, NHG) as gr:
                for k4 in range(KH):
                    pe.wait_ge(h_ready, gr * KH + k4 + 1)
                    for k in range(KD):
                        last = t_.matmul((pA, pB)[k4 % 2][:, 0:HG], w1l[:, k, k4 * P:(k4 + 1) * P],
                                         aggT[:, k, ds(gr * HG, HG)], start=k == 0, stop=k == KD - 1)
                    last.then_inc(h_done, 1)
            pe.wait_ge(h_ready, S3_STEPS + 2)

            def z_tile(t, s):
                pe.wait_ge(z_copied, t + 1)
                for k in range(KH):
                    last = t_.matmul((pC, pD)[s][:, 0:D], hT[:, k, t * P:(t + 1) * P], w2l[:, k, :], start=k == 0,
                                     stop=k == KH - 1)
                last.then_inc(z_done, 1)
            for r in range(NT // 2):
                for s in range(2):
                    z_tile(r * 2 + s, s)
            z_tile(NT - 1, 0)
            pe.sem_inc(r_added, 1)
            for t in range(NT):
                pe.wait_ge(r_added, t + 1)
                for k in range(KH):
                    t_.matmul(pE[:, 0:D], hT[:, k, t * P:(t + 1) * P], w2r[:, k, :], start=k == 0, stop=False)
                t_.matmul(pE[:, 0:D], ones[0:1, :], b2_row, start=False, stop=True).then_inc(r_done, 1)
                items(t * R_ITEMS, R_ITEMS, 1)
            with pe.Fori(0, (ITEMS - R_BASE) // 2) as q:
                items(q * 2 + R_BASE, 2, 1)

            pe.sem_inc(logit_done, 2)

            def gate(t, s):
                pe.wait_ge(x2n_ready, t + 1)
                pe.wait_ge(x2T_ready, t + 1)
                for k in range(KD):
                    last = t_.transpose((pC, pD)[s][:, k * P:(k + 1) * P],
                                        x2n[:, t, k * P:(k + 1) * P], ident[:, :])
                last.then_inc(x2_turned, 1)
                pe.wait_ge(x2T_ready, t + 3)
                for k in range(KD):
                    t_.matmul(pF[:, t * EXP:(t + 1) * EXP], x2T[:, s, k * P:(k + 1) * P], wg[:, k, :], start=k == 0, stop=False)
                t_.matmul(pF[:, t * EXP:(t + 1) * EXP], ones[0:1, :], bg_row, start=False, stop=True).then_inc(logit_done, 1)
            for r in range(NT // 2):
                for s in range(2):
                    gate(r * 2 + s, s)
            gate(NT - 1, 0)
            pe.wait_ge(route, ROUTE_MEMBERS)
            t_.matmul(pA[:, 0:R8], tri[:, :], rt[:, 0, :], start=True, stop=True).then_inc(route_pe, 1)
            t_.matmul(pB[:, 0:R8], ones[:, :], rt[:, 0, :], start=True, stop=True).then_inc(route_pe, 1)

            pe.wait_ge(route, ROUTE_DONE)
            pe.wait_ge(ffw_loaded, 32 * EXP)
            pe.wait_ge(b2_loaded, 16)
            pe.sem_inc(up_done, 2)
            pe.sem_inc(down_done, 2)

            def turn_x(b, s, first=False):
                if not first:
                    pe.wait_ge(xT_ready, b)
                for k in range(KD):
                    last = t_.transpose(bankX[:, k * P:(k + 1) * P], xt[:, s, k * P:(k + 1) * P], ident[:, :])
                last.then_inc(xt_turned, 1)

            def up(b, s, e):
                pe.wait_ge(xT_ready, b + 1)
                for half in range(2):
                    cols_ = slice(half * 512, (half + 1) * 512)
                    t_.matmul(bankH[s][:, cols_], ones_b[:, :], b1_p[:, s, cols_], start=True, stop=False)
                    for k in range(KD):
                        last = t_.matmul(bankH[s][:, cols_], xT[:, s, k * P:(k + 1) * P],
                                         ffw1[:, ds(e, 1), k, cols_].rearrange("p a n -> p (a n)"), start=False, stop=k == KD - 1)
                last.then_inc(up_done, 1)

            def turn_h(b, s, first=False):
                pe.wait_ge(act_done, b + 1)
                if not first:
                    pe.wait_ge(hsT_ready, b)
                for k in range(KF):
                    last = t_.transpose(bankT[:, k * P:(k + 1) * P], hs[:, s, k * P:(k + 1) * P], ident[:, :])
                last.then_inc(hs_turned, 1)

            def down(b, s, e):
                pe.wait_ge(hsT_ready, b + 1)
                pe.wait_ge(y_copied, b + 1)
                t_.matmul(bankY[:, 0:D], ones_b[:, :], b2_p[:, ds(e * D, D)], start=True, stop=False)
                for k in range(KF):
                    last = t_.matmul(bankY[:, 0:D], hsT[:, s, k * P:(k + 1) * P], ffw2[:, ds(e, 1), k, :].rearrange("p a n -> p (a n)"),
                                     start=False, stop=k == KF - 1)
                last.then_inc(down_done, 1)

            def expert(b):
                return pe.value_load(tab_e[0:1, ds(b, 1)], min_val=0, max_val=EXP - 1)
            pe.wait_ge(xt_loaded[0], 16)
            turn_x(0, 0, True)
            pe.wait_ge(bp_loaded[0], 16)
            up(0, 0, expert(0))
            pe.wait_ge(xt_loaded[1], 16)
            turn_x(1, 1)
            pe.wait_ge(bp_loaded[1], 16)
            up(1, 1, expert(1))
            pe.wait_ge(xt_loaded[0], 32)
            turn_x(2, 0)
            turn_h(0, 0, True)
            with pe.Fori(1, NBLK // 2) as r:
                for s in range(2):
                    b = r * 2 + s
                    pe.wait_ge(bp_loaded[s], r * 16 + 16)
                    pe.wait_ge(act_done, b - 1)
                    up(b, s, expert(b))
                    pe.wait_ge(xt_loaded[1 - s], r * 16 + 16 + s * 16)
                    turn_x(b + 1, 1 - s)
                    turn_h(b - 1, 1 - s)
                    down(b - 2, s, expert(b - 2))
            turn_h(NBLK - 1, 1)
            down(NBLK - 2, 0, expert(NBLK - 2))
            down(NBLK - 1, 1, expert(NBLK - 1))


ROUTE_EXP = 13
ROUTE_MEMBERS = 15
ROUTE_POS = 42
ROUTE_DONE = 51
N_W_LOADS = 11


def kernel(x, src, dst, L0_gnn_W1l, L0_gnn_b1l, L0_gnn_W1r, L0_gnn_W2l, L0_gnn_b2l, L0_gnn_W2r, L0_mix_wq,
           L0_mix_bq, L0_mix_wk, L0_mix_bk, L0_mix_wv, L0_mix_bv, L0_mix_wo, L0_mix_bo, L0_ffn_Wg, L0_ffn_bg,
           L0_ffn_W1, L0_ffn_b1, L0_ffn_W2, L0_ffn_b2):
    import concourse.bacc as bacc
    from concourse.bass_utils import run_bass_kernel_spmd as run

    def arr(a):
        return np.ascontiguousarray(np.asarray(a))

    def edges(a, pad):
        a = np.asarray(a)
        return arr(np.concatenate([a, np.full(NC * P - E_ALL, pad, a.dtype)]).reshape(NC, P).T)

    def on_partitions(a):
        return np.asarray(a).reshape(-1, P).T
    data = {
        "x": arr(x),
        "src": edges(src, 0),
        "dst": edges(dst, NP),
        "wq": arr(L0_mix_wq),
        "wkv": arr(np.concatenate([np.asarray(L0_mix_wk), np.asarray(L0_mix_wv)], axis=1)),
        "wo": arr(L0_mix_wo),
        "w1l": arr(np.asarray(L0_gnn_W1l).T),
        "w1r": arr(np.asarray(L0_gnn_W1r).T),
        "w2l": arr(np.asarray(L0_gnn_W2l).T),
        "w2r": arr(np.asarray(L0_gnn_W2r).T),
        "rows": arr(np.concatenate([np.asarray(a) for a in (L0_mix_bk, L0_mix_bv, L0_mix_bo, L0_gnn_b2l,
                                                            L0_ffn_bg)]).reshape(1, -1)),
        "cols": arr(np.concatenate([on_partitions(L0_mix_bq), on_partitions(L0_gnn_b1l)], axis=1)),
        "ffw1": arr(L0_ffn_W1),
        "ffw2": arr(L0_ffn_W2),
        "ffb": arr(np.concatenate([np.asarray(L0_ffn_b1).reshape(-1), np.asarray(L0_ffn_b2).reshape(-1)])),
        "wg": arr(L0_ffn_Wg),
    }
    nc = bacc.Bacc("TRN2", target_bir_lowering=False, num_devices=1)
    args = [nc.dram_tensor(f"in_{name}", a.shape, mybir.dt.from_np(a.dtype), kind="ExternalInput").ap()
            for name, a in data.items()]
    out = nc.dram_tensor("out", (N_NODES, D), mybir.dt.float32, kind="ExternalOutput").ap()
    program(nc, *args, out)
    r = run(nc, [{f"in_{name}": a for name, a in data.items()}], core_ids=[0])
    return r.results[0]["out"]
```
